# Optimizing a Trainium2 kernel written in Bass

```python
import numpy as np
import jax
import jax.numpy as jnp

def _softmax(x, axis=-1):
    return jax.nn.softmax(x, axis=axis)

def _gelu(x):
    return jax.nn.gelu(x, approximate=True)

def _silu(x):
    return jax.nn.silu(x)

def _sigmoid(x):
    return jax.nn.sigmoid(x)

def _layernorm(x, axis=-1, eps=1e-05):
    m = jnp.mean(x, axis=axis, keepdims=True)
    v = jnp.var(x, axis=axis, keepdims=True)
    return (x - m) / jnp.sqrt(v + eps)

def _scatter_add(tgt, idx, src, axis=0):
    return tgt.at[idx].add(src)

def _segment_sum(src, seg, n):
    return jax.ops.segment_sum(src, seg, n)
kernel_name = 'mk_adj_resnorm_d2_adj_r2_705a81'

def setup_inputs(seed: int=0):
    np.random.seed(seed)
    _w = jnp.asarray

    def _rec_inputs():
        import jax
        import jax.numpy as jnp
        _gk = jax.random.key(seed)
        x = -0.0003929 + 0.9999 * jax.random.normal(jax.random.fold_in(_gk, 1), (16, 512, 256), jnp.float32)
        _a = jax.random.bernoulli(jax.random.fold_in(_gk, 2), 0.0078125, (512, 512))
        _a = jnp.logical_or(_a, jnp.swapaxes(_a, -1, -2))
        _a = jnp.logical_or(_a, jnp.eye(512, dtype=bool))
        _af = _a.astype(jnp.float32)
        _af = _af * jax.random.uniform(jax.random.fold_in(_gk, 3), (512, 512), jnp.float32, 0.05, 1)
        adj = _af
        return (x, adj)
    x, adj = _rec_inputs()

    def _L0_gnn_setup():
        import jax, jax.numpy as jnp
        import numpy as np
        B, N, F_IN, F_OUT = (16, 1024, 256, 256)
        key = jax.random.key(seed)
        k1, k2, k3 = jax.random.split(key, 3)
        x = jax.random.normal(k1, (B, N, F_IN), dtype=jnp.float32)
        adj = jax.random.uniform(k2, (N, N), dtype=jnp.float32)
        bound = np.sqrt(6.0 / F_OUT)
        weight = jax.random.uniform(k3, (F_IN, F_OUT), dtype=jnp.float32, minval=-bound, maxval=bound)
        bias = jnp.zeros((F_OUT,), dtype=jnp.float32)
        return {'x': x, 'adj': adj, 'weight': weight, 'bias': bias}
    _L0_gnn_all = _L0_gnn_setup()
    _L0_gnn_in = {k: v for k, v in _L0_gnn_all.items() if k in ('weight', 'bias')}
    del _L0_gnn_all

    def _L1_gnn_setup():
        import jax, jax.numpy as jnp
        import numpy as np
        B, N, D, H = (16, 1025, 256, 8)
        LN_EPS = 1e-05

        def _make_mask(key, n):
            n_proto = n - 1
            adj = jax.random.bernoulli(key, 0.03, (n_proto, n_proto)).astype(jnp.float32)
            adj = jnp.clip(adj + adj.T + jnp.eye(n_proto, dtype=jnp.float32), 0.0, 1.0)
            mask = jnp.zeros((n, n), dtype=jnp.float32)
            mask = mask.at[0, :].set(1.0).at[:, 0].set(1.0)
            mask = mask.at[1:, 1:].set(adj)
            return mask
        key = jax.random.key(seed)
        ks = jax.random.split(key, 7)
        s = 1.0 / np.sqrt(D)
        return {'x': jax.random.normal(ks[0], (B, N, D), dtype=jnp.float32), 'w_qkv': jax.random.uniform(ks[1], (D, 3 * D), dtype=jnp.float32, minval=-s, maxval=s), 'w_proj': jax.random.uniform(ks[2], (D, D), dtype=jnp.float32, minval=-s, maxval=s), 'b_proj': jnp.zeros((D,), dtype=jnp.float32), 'ln_gamma': jnp.ones((D,), dtype=jnp.float32), 'ln_beta': jnp.zeros((D,), dtype=jnp.float32), 'attn_mask': _make_mask(ks[3], N)}
    _L1_gnn_all = _L1_gnn_setup()
    _L1_gnn_in = {k: v for k, v in _L1_gnn_all.items() if k in ('w_qkv', 'w_proj', 'b_proj', 'ln_gamma', 'ln_beta')}
    del _L1_gnn_all
    return {'x': x, 'adj': adj, 'L0_gnn_weight': _L0_gnn_in['weight'], 'L0_gnn_bias': _L0_gnn_in['bias'], 'L1_gnn_w_qkv': _L1_gnn_in['w_qkv'], 'L1_gnn_w_proj': _L1_gnn_in['w_proj'], 'L1_gnn_b_proj': _L1_gnn_in['b_proj'], 'L1_gnn_ln_gamma': _L1_gnn_in['ln_gamma'], 'L1_gnn_ln_beta': _L1_gnn_in['ln_beta']}

def reference(x, adj, L0_gnn_weight, L0_gnn_bias, L1_gnn_w_qkv, L1_gnn_w_proj, L1_gnn_b_proj, L1_gnn_ln_gamma, L1_gnn_ln_beta):
    import jax
    import jax.numpy as jnp

    def _L0_gnn_ref(x, adj, weight, bias):
        import jax, jax.numpy as jnp
        import numpy as np
        B, N, F_IN, F_OUT = (16, 1024, 256, 256)
        deg = adj.sum(axis=1)
        deg_inv_sqrt = jnp.where(deg > 0, jax.lax.rsqrt(deg), 0.0)
        norm_adj = adj * deg_inv_sqrt[:, None] * deg_inv_sqrt[None, :]
        support = jnp.einsum('bni,io->bno', x, weight)
        output = jnp.einsum('nm,bmo->bno', norm_adj, support)
        return output + bias

    def _L1_gnn_ref(x, w_qkv, w_proj, b_proj, ln_gamma, ln_beta, attn_mask):
        import jax, jax.numpy as jnp
        import numpy as np
        B, N, D, H = (16, 1025, 256, 8)
        LN_EPS = 1e-05

        def _make_mask(key, n):
            n_proto = n - 1
            adj = jax.random.bernoulli(key, 0.03, (n_proto, n_proto)).astype(jnp.float32)
            adj = jnp.clip(adj + adj.T + jnp.eye(n_proto, dtype=jnp.float32), 0.0, 1.0)
            mask = jnp.zeros((n, n), dtype=jnp.float32)
            mask = mask.at[0, :].set(1.0).at[:, 0].set(1.0)
            mask = mask.at[1:, 1:].set(adj)
            return mask
        b, n, d = x.shape
        hd = d // H
        scale = hd ** (-0.5)
        qkv = (x @ w_qkv).reshape(b, n, 3, H, hd).transpose(2, 0, 3, 1, 4)
        q, k, v = (qkv[0], qkv[1], qkv[2])
        attn = jnp.einsum('bhnd,bhmd->bhnm', q, k) * scale
        attn = jnp.where(attn_mask[None, None] == 0, -jnp.inf, attn)
        attn = jax.nn.softmax(attn, axis=-1)
        o = jnp.einsum('bhnm,bhmd->bhnd', attn, v).transpose(0, 2, 1, 3).reshape(b, n, d)
        o = o @ w_proj + b_proj
        mu = jnp.mean(o, axis=-1, keepdims=True)
        var = jnp.mean(jnp.square(o - mu), axis=-1, keepdims=True)
        ln = (o - mu) * jax.lax.rsqrt(var + LN_EPS) * ln_gamma + ln_beta
        return o + ln
    x = _layernorm(x + _L0_gnn_ref(x, adj, L0_gnn_weight, L0_gnn_bias), axis=-1)
    x = _layernorm(x + _L1_gnn_ref(x, L1_gnn_w_qkv, L1_gnn_w_proj, L1_gnn_b_proj, L1_gnn_ln_gamma, L1_gnn_ln_beta, adj), axis=-1)
    return x

_drawn_inputs = setup_inputs


def setup_inputs(seed=0):
    import zlib

    import numpy as np

    out = dict(_drawn_inputs(seed))
    spreads = {'L0_gnn_bias': (0.0, 0.1),
     'L1_gnn_b_proj': (0.0, 0.1),
     'L1_gnn_ln_gamma': (1.0, 0.2),
     'L1_gnn_ln_beta': (0.0, 0.1)}
    factors = {}
    for name, (base, spread) in spreads.items():
        noise = np.random.default_rng([zlib.crc32(name.encode()), seed]).standard_normal(out[name].shape)
        drawn = base * np.exp(spread * noise) if base else spread * noise
        out[name] = jnp.asarray(drawn.astype(out[name].dtype))
    for name, factor in factors.items():
        out[name] = (out[name] * factor).astype(out[name].dtype)
    return out
```

```python
import concourse.bass as bass
from concourse import mybir
from contextlib import ExitStack


def gcn_attention_resnorm_kernel(nc: bass.Bass, x, adj, w_gcn, b_gcn, w_qkv, w_proj, b_proj, ln_gamma, ln_beta, out):
    f32, f32r, bf16, i32 = mybir.dt.float32, mybir.dt.float32r, mybir.dt.bfloat16, mybir.dt.int32
    ALU, ACT, AX = mybir.AluOpType, mybir.ActivationFunctionType, mybir.AxisListType

    B, N, D = x.shape
    P = 128
    T = N // P
    C = D // P
    HD = 32
    G = C
    J = P // HD
    H = G * J
    SCALE = float(HD) ** -0.5
    EPS = 1e-5
    NEG = -1e30
    KS = 3 * HD
    KC = KS + 2
    SLOTS = 16
    QUAD = J * T
    TILES = G * QUAD
    UNITS = TILES // 2
    MS_RING, PT_RING = 4, 4
    LN1_STEPS, LN2_STEPS = 12, 33
    LOADS = 3 * 16

    x_v = x.rearrange("b (t p) i -> b p t i", p=P)
    out_v = out.rearrange("b (t p) i -> b p t i", p=P)

    def minus(b, k):
        return b - k if isinstance(b, int) else (b[0], b[1] - k)

    def live(b):
        return not isinstance(b, int) or 0 <= b < B

    def parity(b):
        return (b if isinstance(b, int) else b[1]) % 2

    def index(b):
        return b if isinstance(b, int) else b[0] * 2 + b[1]

    def upto(per, b, k):
        return per * b + k if isinstance(b, int) else b[0] * (2 * per) + (per * b[1] + k)

    def upto_parity(per, b, k):
        return per * (b // 2) + k if isinstance(b, int) else b[0] * per + (per * (b[1] // 2) + k)

    def wait(eng, sem, value):
        if not isinstance(value, int) or value > 0:
            eng.wait_ge(sem, value)

    with ExitStack() as ctx:
        def sb(name, shape, dt=f32):
            return ctx.enter_context(nc.sbuf_tensor(name, shape, dt))

        def sem(name):
            return ctx.enter_context(nc.semaphore(name))

        at_hi, at_lo = (sb(f"at_{p}", [P, T, N], f32r) for p in ("hi", "lo"))
        negmask = sb("negmask", [P, T, N], bf16)
        keep_t = sb("keep_t", [P, T, N], i32)
        wg_hi, wg_lo = (sb(f"wg_{p}", [P, C, D], f32r) for p in ("hi", "lo"))
        wq_hi, wq_lo = (sb(f"wq_{p}", [P, C, 3 * D], f32r) for p in ("hi", "lo"))
        wp_hi, wp_lo = (sb(f"wp_{p}", [P, C, D], f32r) for p in ("hi", "lo"))
        bias_rows = sb("bias_rows", [KS, 2, D], f32r)
        bias_sel = sb("bias_sel", [KS, P], f32r)
        ident, ident_r = sb("ident", [P, P]), sb("ident_r", [P, P], f32r)
        gamma, beta = sb("gamma", [P, D]), sb("beta", [P, D])
        x_raw = sb("x_raw", [P, T, D])
        x_hi, x_lo = (sb(f"x_{p}", [P, T, D], f32r) for p in ("hi", "lo"))
        tr_hi, tr_lo = (sb(f"tr_{p}", [P, C, N], f32r) for p in ("hi", "lo"))
        y = sb("y", [P, 2, T, D])
        yb = sb("yb", [P, 2, T, D])
        stage_hi, stage_lo = (sb(f"stage_{p}", [P, 2, N], f32r) for p in ("hi", "lo"))
        q_stack, k_stack = ([sb(f"{n}_stack{p}", [P, H, N], f32r) for p in range(2)] for n in "qk")
        v = sb("v", [P, 2, T, D])
        neg_s = sb("neg_s", [P, MS_RING, N])
        pt = sb("pt", [P, PT_RING, 2, N])
        ot_hi, ot_lo = (sb(f"ot_{p}", [P, G, N], f32r) for p in ("hi", "lo"))
        o = sb("o", [P, T, D])
        res = sb("res", [P, T, D])
        neg_max = sb("neg_max", [P, 2, TILES])
        sums, ln_sums = sb("sums", [P, TILES]), sb("ln_sums", [P, TILES])
        c_col = sb("c_col", [P, G, QUAD])
        c_hi, c_lo = (sb(f"c_{p}", [QUAD, P], f32r) for p in ("hi", "lo"))
        stats = [sb(f"stats{n}", [P, T, 6]) for n in range(3)]
        mean_var = [sb(f"mean_var{n}", [P, T, 2]) for n in range(3)]
        var_eps, root, rstd = ([sb(f"{s}{n}", [P, T]) for n in range(3)] for s in ("var_eps", "root", "rstd"))
        adj_raw = pt[:, 0:2, :, :].rearrange("p a b n -> p (a b) n")
        adj_row = pt[:, 2:4, :, :].rearrange("p a b n -> p (a b) n")
        wq_raw = y[:, :, :, :].rearrange("p a t d -> p (a t d)")[:, 0:C * 3 * D].rearrange("p (c d) -> p c d", c=C)
        yb_flat = yb[:, :, :, :].rearrange("p a t d -> p (a t) d")
        wg_raw, wp_raw, bias_raw = yb_flat[:, 0:C, :], yb_flat[:, C:2 * C, :], yb_flat[0:KS, 2 * C:2 * C + 2, :]

        deg, deg_pos, deg_root, d_inv = (sums[:, n * T:(n + 1) * T] for n in range(4))

        ps = ctx.enter_context(nc.psum_tensor("ps", [P, 8, N], f32))
        ST, SA, AV, MISC = 0, 4, 6, 7

        adj_loaded, w_loaded, x_loaded, stored = (sem(n) for n in ("adj_loaded", "w_loaded", "x_loaded", "stored"))
        q_loaded, k_loaded = ([[sem(f"{n}_loaded{p}{g}") for g in range(G)] for p in range(2)] for n in "qk")
        c_loaded = [sem(f"c_loaded{g}") for g in range(G)]
        ident_made, ones_made, deg_step, root_made = (sem(n) for n in ("ident_made", "ones_made", "deg_step", "root_made"))
        adj_t_made, row_t_made, const_step, consts_made = (
            sem(n) for n in ("adj_t_made", "row_t_made", "const_step", "consts_made"))
        z_sum, gcn_sum, yt_made, qk_sum, v_sum, proj_sum = (
            sem(n) for n in ("z_sum", "gcn_sum", "yt_made", "qk_sum", "v_sum", "proj_sum"))
        sa_made, ct_made, st_made, av_made = (sem(n) for n in ("sa_made", "ct_made", "st_made", "av_made"))
        z_hi_set, r_set, yt_hi_set, qk_hi_set, v_set, o_set = (
            sem(n) for n in ("z_hi_set", "r_set", "yt_hi_set", "qk_hi_set", "v_set", "o_set"))
        row_exp, ln_sum_set, c_hi_set, p_exp, ot_hi_set = (
            sem(n) for n in ("row_exp", "ln_sum_set", "c_hi_set", "p_exp", "ot_hi_set"))
        ln1_root, ln2_root = sem("ln1_root"), sem("ln2_root")
        x_hi_set, x_split, z_lo_set, yt_lo_set, qk_lo_set, ot_lo_set = (
            sem(n) for n in ("x_hi_set", "x_split", "z_lo_set", "yt_lo_set", "qk_lo_set", "ot_lo_set"))
        row_max, c_col_set, c_lo_set, ln1_step, y_set, ln2_step, res_set = (
            sem(n) for n in ("row_max", "c_col_set", "c_lo_set", "ln1_step", "y_set", "ln2_step", "res_set"))
        p_masked, yb_set = sem("p_masked"), sem("yb_set")

        block = ctx.enter_context(nc.Block())

        def run(eng, step):
            for i in range(-2, 4):
                step(i)
            with eng.Fori(0, (B - 6) // 2) as r:
                step((r, 4))
                step((r, 5))
            for i in range(B - 2, B + 2):
                step(i)

        def ahead(eng, value):
            return value if isinstance(value, int) else eng.to_reg(value)

        def score_tile(k):
            return k // QUAD, k % QUAD // J, k % J

        def column(k):
            g, t, j = score_tile(k)
            return g * QUAD + j * T + t

        def unit_of_slot(i, s):
            return (i, s - 12) if s >= 12 else (minus(i, 1), s + 4)

        @block.sync
        def _(sp):
            sp.dma_start(adj_raw, adj.rearrange("(t p) m -> p t m", p=P)).then_inc(adj_loaded, 16)
            sp.dma_start(wg_raw, w_gcn.rearrange("(c p) d -> p c d", p=P)).then_inc(w_loaded, 16)
            sp.dma_start(wp_raw, w_proj.rearrange("(c p) d -> p c d", p=P)).then_inc(w_loaded, 16)
            sp.dma_start(wq_raw, w_qkv.rearrange("(c p) d -> p c d", p=P)).then_inc(w_loaded, 16)
            for n, row in enumerate((b_gcn, b_proj)):
                sp.dma_start(bias_raw[:, n, :], row.partition_broadcast(KS)).then_inc(w_loaded, 16)
            for tile, row in ((gamma, ln_gamma), (beta, ln_beta)):
                sp.dma_start(tile[:, :], row.partition_broadcast(P)).then_inc(w_loaded, 16)

            def load_x(b):
                if live(b):
                    free = ahead(sp, upto(1, b, 0))
                    sp.wait_ge(adj_loaded, 16)
                    wait(sp, x_split, free)
                    sp.dma_start(x_raw[:, :, :], x_v[index(b)]).then_inc(x_loaded, 16)

            def load_c(b, g):
                if live(b):
                    sp.wait_ge(c_lo_set, upto(G, b, g + 1))
                    for n, part in enumerate((c_hi, c_lo)):
                        row = q_stack[parity(b)][KS + n:KS + n + 1, g * J:(g + 1) * J, :]
                        sp.dma_start(row.rearrange("o j (t p) -> o (j t) p", p=P).bitcast(f32),
                                     part[:, :].bitcast(f32)).then_inc(c_loaded[g], 16)

            def load_stack(b, g, which):
                if live(b):
                    split = ahead(sp, upto(2 * G, b, 2 * g + which + 1))
                    free = ahead(sp, upto(UNITS, minus(b, 2), (g + 1) * UNITS // G))
                    sp.wait_ge(qk_lo_set, split)
                    wait(sp, st_made, free)
                    stack = (q_stack, k_stack)[which][parity(b)]
                    done = (q_loaded, k_loaded)[which][parity(b)][g]
                    parts = ((stage_hi, stage_lo, stage_hi), (stage_hi, stage_hi, stage_lo))[which]
                    for n, part in enumerate(parts):
                        sp.dma_start(stack[n * HD:(n + 1) * HD, g * J:(g + 1) * J, :].bitcast(f32),
                                     part[:, which, :].bitcast(f32)).then_inc(done, 16)

            def store(b):
                if live(b):
                    given = ahead(sp, upto(T, b, T))
                    sp.wait_ge(adj_loaded, 16)
                    sp.wait_ge(res_set, given)
                    sp.dma_start(out_v[index(b)], res[:, :, :]).then_inc(stored, 16)

            def step(i):
                load_c(minus(i, 1), 1)
                load_c(i, 0)
                load_stack(minus(i, -1), 0, 0)
                store(minus(i, 2))
                load_stack(minus(i, -1), 0, 1)
                load_x(minus(i, -2))
                load_stack(minus(i, -1), 1, 0)
                load_stack(minus(i, -1), 1, 1)

            run(sp, step)
            sp.wait_ge(stored, 16 * B)

        @block.tensor
        def _(pe):
            def split_sum(dst, pairs, first=True):
                terms = [(a, b) for (ah, al), (bh, bl) in pairs for a, b in ((ah, bh), (al, bh), (ah, bl))]
                for n, (a, b) in enumerate(terms):
                    last = nc.tensor.matmul(dst, a, b, start=first and n == 0, stop=n == len(terms) - 1)
                return last

            pe.wait_ge(ident_made, 2)
            pe.wait_ge(adj_loaded, 16)
            for m in range(T):
                for t in range(T):
                    last = nc.tensor.transpose(ps[:, m, t * P:(t + 1) * P], adj_raw[:, t, m * P:(m + 1) * P], ident[:, :])
            last.then_inc(adj_t_made, 1)
            pe.wait_ge(const_step, T)
            for m in range(T):
                for t in range(T):
                    last = nc.tensor.transpose(ps[:, 4 + m, t * P:(t + 1) * P], adj_row[:, t, m * P:(m + 1) * P], ident[:, :])
            last.then_inc(row_t_made, 1)
            pe.wait_ge(consts_made, 1)
            pe.wait_ge(ones_made, 5)

            def aggregate(b, c):
                if live(b):
                    if c == 0:
                        pe.wait_ge(x_split, upto(1, b, 1))
                        wait(pe, v_set, upto(2, minus(b, 1), 2))
                        wait(pe, o_set, upto(2, minus(b, 3), 2))
                    else:
                        pe.wait_ge(z_lo_set, upto(C, b, c))
                    cols = slice(c * P, (c + 1) * P)
                    split_sum(ps[:, MISC, :], [((x_hi[:, t, cols], x_lo[:, t, cols]), (at_hi[:, t, :], at_lo[:, t, :]))
                                               for t in range(T)]).then_inc(z_sum, 1)

            def gcn(b, h):
                if live(b):
                    if h == 0:
                        pe.wait_ge(z_lo_set, upto(C, b, C))
                    else:
                        pe.wait_ge(r_set, upto(2, b, h))
                    for n in range(2):
                        t = 2 * h + n
                        rows, dst = slice(t * P, (t + 1) * P), ps[:, MISC, n * D:(n + 1) * D]
                        nc.tensor.matmul(dst, bias_sel[:, :], bias_rows[:, 0, :], start=True, stop=False)
                        nc.tensor.matmul(dst, ident_r[:, :], x_hi[:, t, :], start=False, stop=False)
                        nc.tensor.matmul(dst, ident_r[:, :], x_lo[:, t, :], start=False, stop=False)
                        last = split_sum(dst, [((tr_hi[:, c, rows], tr_lo[:, c, rows]), (wg_hi[:, c, :], wg_lo[:, c, :]))
                                               for c in range(C)], first=False)
                    last.then_inc(gcn_sum, 1)

            def transpose_y(b, c):
                if live(b):
                    if c == 0:
                        pe.wait_ge(y_set, upto(T, b, T))
                    else:
                        pe.wait_ge(yt_lo_set, upto(C, b, c))
                    for t in range(T):
                        last = nc.tensor.transpose(ps[:, MISC, t * P:(t + 1) * P],
                                                   y[:, parity(b), t, c * P:(c + 1) * P], ident[:, :])
                    last.then_inc(yt_made, 1)

            def queries_keys(b, g, which):
                if live(b):
                    if g == 0 and which == 0:
                        pe.wait_ge(yt_lo_set, upto(C, b, C))
                    else:
                        pe.wait_ge(qk_lo_set, upto(2 * G, b, 2 * g + which))
                    cols = slice(which * D + g * P, which * D + (g + 1) * P)
                    split_sum(ps[:, MISC, :], [((wq_hi[:, c, cols], wq_lo[:, c, cols]), (tr_hi[:, c, :], tr_lo[:, c, :]))
                                               for c in range(C)]).then_inc(qk_sum, 1)

            def values(b, h):
                if live(b):
                    if h == 0:
                        pe.wait_ge(qk_lo_set, upto(2 * G, b, 2 * G))
                    else:
                        pe.wait_ge(v_set, upto(2, b, h))
                    for n in range(2):
                        rows = slice((2 * h + n) * P, (2 * h + n + 1) * P)
                        last = split_sum(ps[:, MISC, n * D:(n + 1) * D],
                                         [((tr_hi[:, c, rows], tr_lo[:, c, rows]),
                                           (wq_hi[:, c, 2 * D:3 * D], wq_lo[:, c, 2 * D:3 * D])) for c in range(C)])
                    last.then_inc(v_sum, 1)

            def project(b, h):
                if live(b):
                    if h == 0:
                        pe.wait_ge(ot_lo_set, upto(G, b, G))
                        wait(pe, v_set, min(2 * (b + 3), 2 * B) if isinstance(b, int) else upto(2, b, 6))
                    else:
                        pe.wait_ge(o_set, upto(2, b, h))
                    for n in range(2):
                        rows, dst = slice((2 * h + n) * P, (2 * h + n + 1) * P), ps[:, MISC, n * D:(n + 1) * D]
                        nc.tensor.matmul(dst, bias_sel[:, :], bias_rows[:, 1, :], start=True, stop=False)
                        last = split_sum(dst, [((ot_hi[:, c, rows], ot_lo[:, c, rows]), (wp_hi[:, c, :], wp_lo[:, c, :]))
                                               for c in range(C)], first=False)
                    last.then_inc(proj_sum, 1)

            def wait_turn(b, turn):
                before = turn - 2
                if before == 4:
                    wait(pe, c_lo_set, upto(G, minus(b, 1), 2))
                elif before == 21:
                    wait(pe, c_lo_set, upto(G, b, 1))
                else:
                    tile = before if before < 4 else before - 1 if before < 21 else before - 2
                    value = upto(TILES, b, tile + 1)
                    wait(pe, row_max, min(value, TILES * B) if isinstance(value, int) else value)

            def score(b, k):
                if live(b):
                    g, t, j = score_tile(k)
                    if k % QUAD == 0:
                        pe.wait_ge(q_loaded[parity(b)][g], upto_parity(LOADS, b, LOADS))
                        pe.wait_ge(k_loaded[parity(b)][g], upto_parity(LOADS, b, LOADS))
                    turn = k if k < 4 else k + 1 if k < 20 else k + 2
                    wait_turn(b, turn)
                    nc.tensor.matmul(ps[:, SA + turn % 2, :], q_stack[parity(b)][0:KS, g * J + j, t * P:(t + 1) * P],
                                     k_stack[parity(b)][0:KS, g * J + j, :], start=True, stop=True).then_inc(sa_made, 1)

            def transpose_c(b, g):
                if live(b):
                    turn = (21, 4)[g]
                    pe.wait_ge(c_col_set, upto(G, b, g + 1))
                    wait_turn(minus(b, -g), turn)
                    nc.tensor.transpose(ps[0:QUAD, SA + turn % 2, 0:P], c_col[:, g, :], ident[:, :]).then_inc(ct_made, 1)

            def score_t(b, u):
                if live(b):
                    g, m, p = u // (2 * T), u // 2 % T, u % 2
                    if u % (2 * T) == 0:
                        pe.wait_ge(c_loaded[g], upto(32, b, 32))
                    wait(pe, p_exp, upto(UNITS, b, u - 1))
                    for n in range(2):
                        h = g * J + 2 * p + n
                        last = nc.tensor.matmul(ps[:, ST + u % 2 * 2 + n, :], k_stack[parity(b)][0:KC, h, m * P:(m + 1) * P],
                                                q_stack[parity(b)][0:KC, h, :], start=True, stop=True)
                    last.then_inc(st_made, 1)

            def weigh(b, g, m):
                if live(b):
                    if m == 0:
                        wait(pe, ot_lo_set, upto(G, b, g))
                        pe.wait_ge(v_set, upto(2, b, 2))
                    pe.wait_ge(p_masked, upto(UNITS, b, g * 2 * T + 2 * m + 2))
                    for j in range(J):
                        u = 2 * m + j // 2
                        h = g * J + j
                        last = nc.tensor.matmul(ps[j * HD:(j + 1) * HD, AV, :], v[:, parity(b), m, h * HD:(h + 1) * HD],
                                                pt[:, u % PT_RING, j % 2, :], start=m == 0, stop=m == T - 1)
                    last.then_inc(av_made, 1)

            def step(i):
                front, back = minus(i, -1), minus(i, 2)
                for s in range(SLOTS):
                    score_t(*unit_of_slot(i, s))
                    score(i, 2 * s)
                    score(i, 2 * s + 1)
                    if s % 2 == 1:
                        n = (s - 15) % 16 // 2
                        weigh(i if s == 15 else minus(i, 1), n // T, n % T)
                    if s == 1:
                        transpose_c(minus(i, 1), 1)
                    if s == 9:
                        transpose_c(i, 0)
                    if s in (0, 1):
                        project(back, s)
                    if s in (2, 3):
                        aggregate(front, s - 2)
                    if s in (4, 5):
                        gcn(front, s - 4)
                    if s in (8, 9):
                        transpose_y(front, s - 8)
                    if 10 <= s < 14:
                        queries_keys(front, (s - 10) // 2, s % 2)
                    if s >= 14:
                        values(front, s - 14)

            run(pe, step)

        @block.scalar
        def _(act):
            act.wait_ge(deg_step, 3)
            nc.scalar.activation(deg_root[:, :], deg[:, :], ACT.Sqrt).then_inc(root_made, 1)
            nc.scalar.preload_act_table_set("natural_log_exp_and_others")

            def z_hi(b, c):
                if live(b):
                    act.wait_ge(z_sum, upto(C, b, c + 1))
                    nc.scalar.activation(tr_hi[:, c, :], ps[:, MISC, :], ACT.Copy).then_inc(z_hi_set, 1)

            def r_copy(b, h):
                if live(b):
                    act.wait_ge(gcn_sum, upto(2, b, h + 1))
                    wait(act, yb_set, upto(1, minus(b, 1), 0))
                    nc.scalar.activation(y[:, parity(b), 2 * h:2 * h + 2, :], ps[:, MISC, :], ACT.Copy).then_inc(r_set, 1)

            def yt_hi(b, c):
                if live(b):
                    act.wait_ge(yt_made, upto(C, b, c + 1))
                    nc.scalar.activation(tr_hi[:, c, :], ps[:, MISC, :], ACT.Copy).then_inc(yt_hi_set, 1)

            def qk_hi(b, g, which):
                if live(b):
                    act.wait_ge(qk_sum, upto(2 * G, b, 2 * g + which + 1))
                    loaded = (q_loaded, k_loaded)[which]
                    if g:
                        act.wait_ge(loaded[parity(b)][0], upto_parity(LOADS, b, LOADS))
                    else:
                        wait(act, loaded[1 - parity(b)][G - 1], upto_parity(LOADS, minus(b, 1), LOADS))
                    nc.scalar.activation(stage_hi[:, which, :], ps[:, MISC, :], ACT.Copy,
                                         scale=(SCALE, 1.0)[which]).then_inc(qk_hi_set, 1)

            def v_copy(b, h):
                if live(b):
                    act.wait_ge(v_sum, upto(2, b, h + 1))
                    nc.scalar.activation(v[:, parity(b), 2 * h:2 * h + 2, :], ps[:, MISC, :], ACT.Copy).then_inc(v_set, 1)

            def o_copy(b, h):
                if live(b):
                    act.wait_ge(proj_sum, upto(2, b, h + 1))
                    wait(act, ln2_step, upto(LN2_STEPS, minus(b, 1), 20))
                    nc.scalar.activation(o[:, 2 * h:2 * h + 2, :], ps[:, MISC, :], ACT.Copy).then_inc(o_set, 1)

            def c_round(b, g):
                if live(b):
                    act.wait_ge(ct_made, upto(G, b, g + 1))
                    wait(act, c_loaded[1 - g], upto(32, b, 32 * g))
                    turn = (21, 4)[g]
                    nc.scalar.activation(c_hi[:, :], ps[0:QUAD, SA + turn % 2, 0:P], ACT.Copy).then_inc(c_hi_set, 1)

            def ot_round(b, g):
                if live(b):
                    act.wait_ge(av_made, upto(G * T, b, (g + 1) * T))
                    wait(act, proj_sum, upto(2, b, 0))
                    nc.scalar.activation(ot_hi[:, g, :], ps[:, AV, :], ACT.Copy).then_inc(ot_hi_set, 1)

            def exp_t(b, u):
                if live(b):
                    act.wait_ge(st_made, upto(UNITS, b, u + 1))
                    wait(act, av_made, upto(G * T, b, (u - PT_RING) // 2 + 1))
                    bank = ST + u % 2 * 2
                    nc.scalar.activation(pt[:, u % PT_RING, :, :], ps[:, bank:bank + 2, :], ACT.Exp).then_inc(p_exp, 1)

            def exp_row(b, k):
                if live(b):
                    act.wait_ge(row_max, upto(TILES, b, k + 1))
                    col = slice(column(k), column(k) + 1)
                    nc.scalar.activation(neg_s[:, k % MS_RING, :], neg_s[:, k % MS_RING, :], ACT.Exp, bias=neg_max[:, parity(b), col],
                                         scale=-1.0, accum_out=sums[:, col]).then_inc(row_exp, 1)

            def ln_sum(b, g):
                if live(b):
                    act.wait_ge(row_exp, upto(TILES, b, (g + 1) * QUAD))
                    cols = slice(g * QUAD, (g + 1) * QUAD)
                    nc.scalar.activation(ln_sums[:, cols], sums[:, cols], ACT.Ln).then_inc(ln_sum_set, 1)

            def inverse_root(b, n):
                if live(b):
                    step_sem, root_sem, steps, k, per, at = (
                        (ln1_step, ln1_root, LN1_STEPS, 9, 2, 0), (ln2_step, ln2_root, LN2_STEPS, 9, 4, 0),
                        (ln2_step, ln2_root, LN2_STEPS, 30, 4, 2))[n]
                    act.wait_ge(step_sem, upto(steps, b, k))
                    nc.scalar.activation(root[n][:, :], var_eps[n][:, :], ACT.Ln).then_inc(root_sem, 1)
                    act.wait_ge(root_sem, upto(per, b, at + 1))
                    nc.scalar.activation(root[n][:, :], root[n][:, :], ACT.Exp, scale=-0.5).then_inc(root_sem, 1)

            def step(i):
                front, last, back = minus(i, -1), minus(i, 1), minus(i, 2)
                for s in range(SLOTS):
                    if s == 0:
                        v_copy(i, 1)
                    if s in (1, 2):
                        o_copy(back, s - 1)
                    if s in (3, 4):
                        z_hi(front, s - 3)
                    if s in (5, 6):
                        r_copy(front, s - 5)
                    if s in (9, 10):
                        yt_hi(front, s - 9)
                    if 11 <= s < 15:
                        qk_hi(front, (s - 11) // 2, (s - 11) % 2)
                    if s == 15:
                        v_copy(front, 0)
                    if s == 2:
                        c_round(last, 1)
                    if s == 10:
                        c_round(i, 0)
                    if s in (6, 14):
                        ot_round(last, (s - 6) // 8)
                    if s == 4:
                        inverse_root(back, 1)
                    if s == 7:
                        inverse_root(front, 0)
                    if s == 10:
                        inverse_root(back, 2)
                    exp_t(*unit_of_slot(i, s))
                    for k in (2 * s - 2, 2 * s - 1):
                        exp_row(i if k >= 0 else last, k % TILES)
                    if s == 0:
                        ln_sum(last, 1)
                    if s == 8:
                        ln_sum(i, 0)

            run(act, step)

        @block.vector
        def _(dve):
            deg_n, const_n = [0], [0]

            def deg_link(ins):
                deg_n[0] += 1
                ins.then_inc(deg_step, 1)
                dve.wait_ge(deg_step, deg_n[0])

            dve.wait_ge(adj_loaded, 16)
            deg_link(nc.vector.reduce_sum(d_inv[:, :], adj_raw, axis=AX.X))
            deg_link(nc.vector.tensor_scalar(deg_pos[:, :], d_inv[:, :], 0.0, None, ALU.is_gt))
            deg_link(nc.vector.tensor_scalar_max(deg[:, :], d_inv[:, :], 1e-30))
            nc.vector.tensor_scalar(negmask[:, :, :], adj_raw, 0.0, NEG, ALU.is_equal, ALU.mult)
            dve.wait_ge(root_made, 1)
            deg_link(nc.vector.reciprocal(d_inv[:, :], deg_root[:, :]))
            deg_link(nc.vector.tensor_tensor(deg_root[:, :], d_inv[:, :], d_inv[:, :], ALU.mult))
            deg_link(nc.vector.scalar_tensor_tensor(deg_root[:, :], deg_root[:, :], -0.5, deg[:, :], ALU.mult, ALU.mult))
            deg_link(nc.vector.scalar_tensor_tensor(d_inv[:, :], deg_root[:, :], 1.5, d_inv[:, :], ALU.add, ALU.mult))
            deg_link(nc.vector.tensor_tensor(d_inv[:, :], d_inv[:, :], deg_pos[:, :], ALU.mult))
            for t in range(T):
                nc.vector.tensor_scalar(adj_row[:, t, :], adj_raw[:, t, :], d_inv[:, t:t + 1], None,
                                        ALU.mult).then_inc(const_step, 1)
            const_n[0] = T

            dve.wait_ge(w_loaded, 16 * 7)
            def by_size(w):
                return w[:, :, 0:2 * D].rearrange("p c (g j d) -> p c g d j", j=J, d=HD)

            def halves(w):
                return w[:, :, 0:2 * D].rearrange("p c (g d j) -> p c g d j", j=J, d=HD)

            for hi, lo, raw in [(wg_hi[:, :, :], wg_lo[:, :, :], wg_raw), (wp_hi[:, :, :], wp_lo[:, :, :], wp_raw),
                                (wq_hi[:, :, 2 * D:], wq_lo[:, :, 2 * D:], wq_raw[:, :, 2 * D:])] + [
                                (halves(wq_hi)[:, c, g], halves(wq_lo)[:, c, g], by_size(wq_raw)[:, c, g])
                                for c in range(C) for g in range(2 * G)]:
                nc.vector.tensor_copy(hi, raw).then_inc(const_step, 1)
                const_n[0] += 1
                dve.wait_ge(const_step, const_n[0])
                nc.vector.tensor_tensor(lo, raw, hi.bitcast(f32), ALU.subtract)
            nc.vector.tensor_copy(bias_rows[:, :, :], bias_raw).then_inc(const_step, 1)
            const_n[0] += 1
            dve.wait_ge(const_step, const_n[0])
            nc.vector.tensor_tensor(bias_rows[HD:2 * HD, :, :], bias_raw[HD:2 * HD, :, :],
                                    bias_rows[HD:2 * HD, :, :].bitcast(f32), ALU.subtract)
            dve.wait_ge(ident_made, 2)
            nc.vector.tensor_copy(ident_r[:, :], ident[:, :])
            dve.wait_ge(adj_t_made, 1)
            nc.vector.tensor_scalar(keep_t[:, :, :], ps[:, 0:4, :], 0.0, None, ALU.not_equal)
            dve.wait_ge(row_t_made, 1)
            for m in range(T):
                nc.vector.tensor_scalar(at_hi[:, m, :], ps[:, 4 + m, :], d_inv[:, m:m + 1], None,
                                        ALU.mult).then_inc(const_step, 1)
                const_n[0] += 1
                dve.wait_ge(const_step, const_n[0])
                made = nc.vector.scalar_tensor_tensor(at_lo[:, m, :], ps[:, 4 + m, :], d_inv[:, m:m + 1],
                                                      at_hi[:, m, :].bitcast(f32), ALU.mult, ALU.subtract)
            made.then_inc(consts_made, 1)

            def split_x(b):
                if live(b):
                    dve.wait_ge(x_loaded, upto(16, b, 16))
                    wait(dve, gcn_sum, upto(2, b, 0))
                    nc.vector.tensor_copy(x_hi[:, :, :], x_raw[:, :, :]).then_inc(x_hi_set, 1)
                    dve.wait_ge(x_hi_set, upto(1, b, 1))
                    nc.vector.tensor_tensor(x_lo[:, :, :], x_raw[:, :, :], x_hi[:, :, :].bitcast(f32),
                                            ALU.subtract).then_inc(x_split, 1)

            def remainder(lo, hi, bank):
                return nc.vector.tensor_tensor(lo, ps[:, bank, :], hi.bitcast(f32), ALU.subtract)

            def z_lo(b, c):
                if live(b):
                    dve.wait_ge(z_hi_set, upto(C, b, c + 1))
                    remainder(tr_lo[:, c, :], tr_hi[:, c, :], MISC).then_inc(z_lo_set, 1)

            def yt_lo(b, c):
                if live(b):
                    dve.wait_ge(yt_hi_set, upto(C, b, c + 1))
                    remainder(tr_lo[:, c, :], tr_hi[:, c, :], MISC).then_inc(yt_lo_set, 1)

            def qk_lo(b, g, which):
                if live(b):
                    dve.wait_ge(qk_hi_set, upto(2 * G, b, 2 * g + which + 1))
                    nc.vector.scalar_tensor_tensor(stage_lo[:, which, :], ps[:, MISC, :], (SCALE, 1.0)[which],
                                                   stage_hi[:, which, :].bitcast(f32), ALU.mult,
                                                   ALU.subtract).then_inc(qk_lo_set, 1)

            def ot_lo_part(b, g):
                if live(b):
                    dve.wait_ge(ot_hi_set, upto(G, b, g + 1))
                    remainder(ot_lo[:, g, :], ot_hi[:, g, :], AV).then_inc(ot_lo_set, 1)

            def c_column(b, g):
                if live(b):
                    dve.wait_ge(ln_sum_set, upto(G, b, g + 1))
                    cols = slice(g * QUAD, (g + 1) * QUAD)
                    nc.vector.tensor_tensor(c_col[:, g, :], neg_max[:, parity(b), cols], ln_sums[:, cols],
                                            ALU.subtract).then_inc(c_col_set, 1)

            def c_remainder(b, g):
                if live(b):
                    dve.wait_ge(c_hi_set, upto(G, b, g + 1))
                    turn = (21, 4)[g]
                    nc.vector.tensor_tensor(c_lo[:, :], ps[0:QUAD, SA + turn % 2, 0:P], c_hi[:, :].bitcast(f32),
                                            ALU.subtract).then_inc(c_lo_set, 1)

            def mask_and_max(b, k):
                if live(b):
                    g, t, j = score_tile(k)
                    made, free = ahead(dve, upto(TILES, b, k + 1)), ahead(dve, upto(TILES, b, k - MS_RING + 1))
                    dve.wait_ge(consts_made, 1)
                    dve.wait_ge(sa_made, made)
                    wait(dve, row_exp, free)
                    nc.vector.tensor_tensor_reduce(
                        out=neg_s[:, k % MS_RING, :], in0=ps[:, SA + (k if k < 4 else k + 1 if k < 20 else k + 2) % 2, :],
                        in1=negmask[:, t, :], scale=-1.0, scalar=3e38, op0=ALU.add, op1=ALU.min,
                        accum_out=neg_max[:, parity(b), column(k):column(k) + 1]).then_inc(row_max, 1)

            def tile_stats(n, chain, src, tiles):
                for t in tiles:
                    nc.vector.bn_stats(stats[n][:, t, :], src[:, t, :]).then_inc(chain, 1)

            def finish_stats(n, chain, per, b, k):
                given = ahead(dve, upto(per, b, k))
                dve.wait_ge(consts_made, 1)
                dve.wait_ge(chain, given)
                for t in range(T):
                    nc.vector.bn_aggr(mean_var[n][:, t, :], stats[n][:, t, :]).then_inc(chain, 1)
                dve.wait_ge(chain, upto(per, b, k + T))
                nc.vector.tensor_scalar_add(var_eps[n][:, :], mean_var[n][:, :, 1], EPS).then_inc(chain, 1)

            def newton(n, chain, per, b, k, root_sem, root_value):
                dve.wait_ge(root_sem, root_value)
                nc.vector.tensor_tensor(rstd[n][:, :], root[n][:, :], root[n][:, :], ALU.mult).then_inc(chain, 1)
                dve.wait_ge(chain, upto(per, b, k + 1))
                nc.vector.scalar_tensor_tensor(rstd[n][:, :], rstd[n][:, :], -0.5, var_eps[n][:, :], ALU.mult,
                                               ALU.mult).then_inc(chain, 1)
                dve.wait_ge(chain, upto(per, b, k + 2))
                nc.vector.scalar_tensor_tensor(rstd[n][:, :], rstd[n][:, :], 1.5, root[n][:, :], ALU.add,
                                               ALU.mult).then_inc(chain, 1)
                dve.wait_ge(chain, upto(per, b, k + 3))

            def ln1_stats(b, h):
                if live(b):
                    dve.wait_ge(r_set, upto(2, b, h + 1))
                    tile_stats(0, ln1_step, y[:, parity(b), :, :], (2 * h, 2 * h + 1))
                    if h == 1:
                        finish_stats(0, ln1_step, LN1_STEPS, b, T)

            def ln1_finish(b):
                if live(b):
                    newton(0, ln1_step, LN1_STEPS, b, 9, ln1_root, upto(2, b, 2))
                    for t in range(T):
                        tile = y[:, parity(b), t, :]
                        nc.vector.tensor_scalar(tile, tile, mean_var[0][:, t, 0:1], rstd[0][:, t:t + 1], ALU.subtract,
                                                ALU.mult).then_inc(y_set, 1)

            def ln2_stats(b, h):
                if live(b):
                    dve.wait_ge(o_set, upto(2, b, h + 1))
                    tile_stats(1, ln2_step, o[:, :, :], (2 * h, 2 * h + 1))
                    if h == 1:
                        finish_stats(1, ln2_step, LN2_STEPS, b, T)

            def ln2_rstd(b):
                if live(b):
                    newton(1, ln2_step, LN2_STEPS, b, 9, ln2_root, upto(4, b, 2))

            def ln2_add(b, h):
                if live(b):
                    if h == 0:
                        wait(dve, stored, upto(16, b, 0))
                    for n in range(2):
                        t = 2 * h + n
                        nc.vector.scalar_tensor_tensor(res[:, t, :], o[:, t, :], mean_var[1][:, t, 0:1], gamma[:, :],
                                                       ALU.subtract, ALU.mult).then_inc(ln2_step, 1)
                    for n in range(2):
                        t = 2 * h + n
                        dve.wait_ge(ln2_step, upto(LN2_STEPS, b, 12 + 4 * h + n + 1))
                        nc.vector.scalar_tensor_tensor(res[:, t, :], res[:, t, :], rstd[1][:, t:t + 1], o[:, t, :],
                                                       ALU.mult, ALU.add).then_inc(ln2_step, 1)

            def ln2_residual(b):
                if live(b):
                    dve.wait_ge(ln2_step, upto(LN2_STEPS, b, 20))
                    dve.wait_ge(yb_set, upto(1, b, 1))
                    nc.vector.tensor_tensor(res[:, :, :], res[:, :, :], yb[:, parity(b), :, :], ALU.add).then_inc(ln2_step, 1)

            def ln3_stats(b):
                if live(b):
                    dve.wait_ge(ln2_step, upto(LN2_STEPS, b, 21))
                    tile_stats(2, ln2_step, res[:, :, :], range(T))
                    finish_stats(2, ln2_step, LN2_STEPS, b, 21 + T)

            def ln3_finish(b):
                if live(b):
                    newton(2, ln2_step, LN2_STEPS, b, 30, ln2_root, upto(4, b, 4))
                    for t in range(T):
                        nc.vector.tensor_scalar(res[:, t, :], res[:, t, :], mean_var[2][:, t, 0:1], rstd[2][:, t:t + 1],
                                                ALU.subtract, ALU.mult).then_inc(res_set, 1)

            def step(i):
                front, last, back = minus(i, -1), minus(i, 1), minus(i, 2)
                for s in range(SLOTS):
                    if s in (3, 4):
                        z_lo(front, s - 3)
                    if s in (9, 10):
                        yt_lo(front, s - 9)
                    if 11 <= s < 15:
                        qk_lo(front, (s - 11) // 2, (s - 11) % 2)
                    if s == 1:
                        c_column(last, 1)
                    if s == 9:
                        c_column(i, 0)
                    if s == 2:
                        c_remainder(last, 1)
                    if s == 10:
                        c_remainder(i, 0)
                    if s in (6, 14):
                        ot_lo_part(last, (s - 6) // 8)
                    mask_and_max(i, 2 * s)
                    mask_and_max(i, 2 * s + 1)
                    if s in (2, 3):
                        ln2_stats(back, s - 2)
                    if s == 4:
                        ln2_rstd(back)
                        ln2_add(back, 0)
                    if s in (5, 6):
                        ln1_stats(front, s - 5)
                    if s == 5:
                        ln2_add(back, 1)
                    if s == 7:
                        ln1_finish(front)
                    if s == 8:
                        ln2_residual(back)
                    if s == 9:
                        ln3_stats(back)
                    if s == 10:
                        ln3_finish(back)
                    if s == 14:
                        split_x(minus(i, -2))

            run(dve, step)

        @block.gpsimd
        def _(pool):
            nc.gpsimd.memset(ident[:, :], 0.0).then_inc(ident_made, 1)
            pool.wait_ge(ident_made, 1)
            nc.gpsimd.affine_select(out=ident[:, :], in_=ident[:, :], compare_op=ALU.not_equal, fill=1.0, base=0,
                                    pattern=[[-1, P]], channel_multiplier=1).then_inc(ident_made, 1)
            pool.wait_ge(ident_made, 2)
            nc.gpsimd.memset(bias_sel[:, :].bitcast(f32), 0.0).then_inc(ones_made, 1)
            ones = [k_stack[0][KS:KC, :, :], k_stack[1][KS:KC, :, :], bias_sel[0:1, :], bias_sel[HD:HD + 1, :]]
            for n, rows in enumerate(ones):
                pool.wait_ge(ones_made, n + 1)
                nc.gpsimd.memset(rows.bitcast(f32), 1.0).then_inc(ones_made, 1)
            pool.wait_ge(consts_made, 1)

            def mask(b, u):
                if live(b):
                    m = u // 2 % T
                    pool.wait_ge(p_exp, upto(UNITS, b, u + 1))
                    tile = pt[:, u % PT_RING, :, :].bitcast(i32)
                    nc.gpsimd.tensor_tensor(tile, tile, keep_t[:, m:m + 1, :].to_broadcast([P, 2, N]),
                                            ALU.mult).then_inc(p_masked, 1)

            def add_beta(b):
                if live(b):
                    pool.wait_ge(y_set, upto(T, b, T))
                    wait(pool, ln2_step, upto(LN2_STEPS, minus(b, 2), 21))
                    nc.gpsimd.tensor_tensor(yb[:, parity(b), :, :], y[:, parity(b), :, :],
                                            beta[:, :].unsqueeze(1).to_broadcast([P, T, D]), ALU.add).then_inc(yb_set, 1)

            def step(i):
                for s in range(SLOTS):
                    mask(*unit_of_slot(i, s))
                    if s == 12:
                        add_beta(i)

            run(pool, step)


_INS = ['x', 'adj', 'L0_gnn_weight', 'L0_gnn_bias', 'L1_gnn_w_qkv', 'L1_gnn_w_proj', 'L1_gnn_b_proj',
        'L1_gnn_ln_gamma', 'L1_gnn_ln_beta']


def kernel(**inputs):
    import numpy as _np
    import concourse.bacc as _bacc
    from concourse import mybir as _mybir
    from concourse.bass_utils import run_bass_kernel_spmd as _run

    nc = _bacc.Bacc("TRN2", target_bir_lowering=False, num_devices=1, dynamic_dma_scratch_size=4096)
    arrays, args = {}, []
    for name in _INS:
        a = _np.ascontiguousarray(inputs[name])
        arrays[f"in_{name}"] = a
        args.append(nc.dram_tensor(f"in_{name}", a.shape, _mybir.dt.from_np(a.dtype), kind="ExternalInput").ap())
    shape = arrays["in_x"].shape
    args.append(nc.dram_tensor("out_0", shape, _mybir.dt.float32, kind="ExternalOutput").ap())
    gcn_attention_resnorm_kernel(nc, *args)
    r = _run(nc, [arrays], core_ids=[0])
    return r.results[0]["out_0"]
```

```python
import concourse.bass as bass
from concourse import mybir
from contextlib import ExitStack


def gcn_attention_resnorm_kernel(nc: bass.Bass, x, adj, w_gcn, b_gcn, w_qkv, w_proj, b_proj, ln_gamma, ln_beta, out):
    f32, f32r, bf16, i32 = mybir.dt.float32, mybir.dt.float32r, mybir.dt.bfloat16, mybir.dt.int32
    ALU, ACT, AX = mybir.AluOpType, mybir.ActivationFunctionType, mybir.AxisListType

    B, N, D = x.shape
    P = 128
    T = N // P
    C = D // P
    HD = 32
    G = C
    J = P // HD
    H = G * J
    SCALE = float(HD) ** -0.5
    EPS = 1e-5
    NEG = -1e30
    KS = 3 * HD
    KC = KS + 2
    SLOTS = 16
    QUAD = J * T
    TILES = G * QUAD
    UNITS = TILES // 2
    ST_BANKS = 3
    MS_RING, PT_RING = 4, 4
    LN1_STEPS, LN2_STEPS = 12, 34
    LOADS = 3 * 16

    x_v = x.rearrange("b (t p) i -> b p t i", p=P)
    out_v = out.rearrange("b (t p) i -> b p t i", p=P)

    def minus(b, k):
        return b - k if isinstance(b, int) else (b[0], b[1] - k)

    def live(b):
        return not isinstance(b, int) or 0 <= b < B

    def parity(b):
        return (b if isinstance(b, int) else b[1]) % 2

    def index(b):
        return b if isinstance(b, int) else b[0] * 2 + b[1]

    def upto(per, b, k):
        return per * b + k if isinstance(b, int) else b[0] * (2 * per) + (per * b[1] + k)

    def clipped(per, b, k):
        return min(upto(per, b, k), per * B) if isinstance(b, int) else upto(per, b, k)

    def upto_parity(per, b, k):
        return per * (b // 2) + k if isinstance(b, int) else b[0] * per + (per * (b[1] // 2) + k)

    def wait(eng, sem, value):
        if not isinstance(value, int) or value > 0:
            eng.wait_ge(sem, value)

    with ExitStack() as ctx:
        def sb(name, shape, dt=f32):
            return ctx.enter_context(nc.sbuf_tensor(name, shape, dt))

        def sem(name):
            return ctx.enter_context(nc.semaphore(name))

        at_hi, at_lo = (sb(f"at_{p}", [P, T, N], f32r) for p in ("hi", "lo"))
        negmask = sb("negmask", [P, T, N], bf16)
        keep_t = sb("keep_t", [P, T, N], i32)
        wg_hi, wg_lo = (sb(f"wg_{p}", [P, C, D], f32r) for p in ("hi", "lo"))
        wq_hi, wq_lo = (sb(f"wq_{p}", [P, C, 3 * D], f32r) for p in ("hi", "lo"))
        wp_hi, wp_lo = (sb(f"wp_{p}", [P, C, D], f32r) for p in ("hi", "lo"))
        bias_rows = sb("bias_rows", [KS, 2, D], f32r)
        bias_sel = sb("bias_sel", [KS, P], f32r)
        ident, ident_r = sb("ident", [P, P]), sb("ident_r", [P, P], f32r)
        gamma, beta = sb("gamma", [P, D]), sb("beta", [P, D])
        x_raw = sb("x_raw", [P, 2, D])
        x_hi, x_lo = (sb(f"x_{p}", [P, T, D], f32r) for p in ("hi", "lo"))
        z_hi, z_lo = (sb(f"z_{p}", [P, C, N], f32r) for p in ("hi", "lo"))
        yt_hi, yt_lo = (sb(f"yt_{p}", [P, C, N], f32r) for p in ("hi", "lo"))
        y = sb("y", [P, 2, T, D])
        yb = sb("yb", [P, 2, T, D])
        stage_hi, stage_lo = (sb(f"stage_{p}", [P, 2, N], f32r) for p in ("hi", "lo"))
        q_stack, k_stack = ([sb(f"{n}_stack{p}", [P, H, N], f32r) for p in range(2)] for n in "qk")
        v = sb("v", [P, 2, T, D])
        neg_s = sb("neg_s", [P, MS_RING, N])
        pt = sb("pt", [P, PT_RING, 2, N])
        ot_hi, ot_lo = (sb(f"ot_{p}", [P, G, N], f32r) for p in ("hi", "lo"))
        o = sb("o", [P, T, D])
        res = sb("res", [P, T, D])
        neg_max = sb("neg_max", [P, 2, TILES])
        sums, ln_sums = sb("sums", [P, TILES]), sb("ln_sums", [P, TILES])
        c_col = sb("c_col", [P, QUAD])
        c_parts = sb("c_parts", [P, G, 2, QUAD], f32r)
        c_rows = sb("c_rows", [2 * QUAD, P], f32r)
        stats = [sb(f"stats{n}", [P, T, 6]) for n in range(3)]
        mean_var = [sb(f"mean_var{n}", [P, T, 2]) for n in range(3)]
        var_eps, root, rstd = ([sb(f"{s}{n}", [P, T]) for n in range(3)] for s in ("var_eps", "root", "rstd"))
        adj_raw = pt[:, 0:2, :, :].rearrange("p a b n -> p (a b) n")
        adj_row = pt[:, 2:4, :, :].rearrange("p a b n -> p (a b) n")
        wq_raw = y[:, :, :, :].rearrange("p a t d -> p (a t d)")[:, 0:C * 3 * D].rearrange("p (c d) -> p c d", c=C)
        yb_flat = yb[:, :, :, :].rearrange("p a t d -> p (a t) d")
        wg_raw, wp_raw, bias_raw = yb_flat[:, 0:C, :], yb_flat[:, C:2 * C, :], yb_flat[0:KS, 2 * C:2 * C + 2, :]

        deg, deg_pos, deg_root, d_inv = (sums[:, n * T:(n + 1) * T] for n in range(4))

        ps = ctx.enter_context(nc.psum_tensor("ps", [P, 8, N], f32))
        ST, SA, AV, MISC = 0, 3, 5, 6

        adj_loaded, w_loaded, x_loaded, stored = (sem(n) for n in ("adj_loaded", "w_loaded", "x_loaded", "stored"))
        q_loaded, k_loaded = ([[sem(f"{n}_loaded{p}{g}") for g in range(G)] for p in range(2)] for n in "qk")
        c_loaded = [sem(f"c_loaded{g}") for g in range(G)]
        ident_made, ones_made, deg_step, root_made = (sem(n) for n in ("ident_made", "ones_made", "deg_step", "root_made"))
        adj_t_made, row_t_made, const_step, consts_made = (
            sem(n) for n in ("adj_t_made", "row_t_made", "const_step", "consts_made"))
        w_hi_set, w_lo_set = sem("w_hi_set"), sem("w_lo_set")
        z_sum, gcn_sum, yt_made, qk_sum, v_sum, proj_sum = (
            sem(n) for n in ("z_sum", "gcn_sum", "yt_made", "qk_sum", "v_sum", "proj_sum"))
        sa_made, ct_made, st_made, av_made = (sem(n) for n in ("sa_made", "ct_made", "st_made", "av_made"))
        z_hi_set, r_set, yt_hi_set, qk_hi_set, v_set, o_set = (
            sem(n) for n in ("z_hi_set", "r_set", "yt_hi_set", "qk_hi_set", "v_set", "o_set"))
        row_exp, ln_sum_set, p_exp, ot_hi_set = (
            sem(n) for n in ("row_exp", "ln_sum_set", "p_exp", "ot_hi_set"))
        ln1_root, ln2_root = sem("ln1_root"), sem("ln2_root")
        x_hi_set, x_split, z_lo_set, yt_lo_set, qk_lo_set, ot_lo_set = (
            sem(n) for n in ("x_hi_set", "x_split", "z_lo_set", "yt_lo_set", "qk_lo_set", "ot_lo_set"))
        row_max, c_step, c_rows_set, ln1_step, y_set, ln2_step, res_set = (
            sem(n) for n in ("row_max", "c_step", "c_rows_set", "ln1_step", "y_set", "ln2_step", "res_set"))
        late_masked = sem("late_masked")
        p_masked, yb_set = sem("p_masked"), sem("yb_set")

        block = ctx.enter_context(nc.Block())

        def run(eng, step):
            for i in range(-2, 4):
                step(i)
            with eng.Fori(0, (B - 6) // 2) as r:
                step((r, 4))
                step((r, 5))
            for i in range(B - 2, B + 2):
                step(i)

        def ahead(eng, value):
            return value if isinstance(value, int) else eng.to_reg(value)

        def score_tile(k):
            return k // QUAD, k % QUAD // J, k % J

        def column(k):
            g, t, j = score_tile(k)
            return g * QUAD + j * T + t

        def misc_bank(number):
            return MISC + number % 2

        def st_bank(u, n):
            turn = 2 * u + n
            return ST + turn % ST_BANKS, max(h for h in range(turn - 2 * ST_BANKS, turn)
                                             if h % (2 * UNITS) % ST_BANKS == turn % ST_BANKS)

        def unit_of_slot(i, s):
            return (i, s - 12) if s >= 12 else (minus(i, 1), s + 4)

        def shared(b, u):
            return isinstance(b, int) and b == B - 1 and u >= 4

        def by_head(w):
            return w[:, :, 0:2 * D].rearrange("p c (g j d) -> p c g d j", j=J, d=HD)

        def as_stacked(w):
            return w[:, :, 0:2 * D].rearrange("p c (g d j) -> p c g d j", j=J, d=HD)

        weights = [(as_stacked(wq_hi)[:, c, g], as_stacked(wq_lo)[:, c, g], by_head(wq_raw)[:, c, g])
                   for c in range(C) for g in range(2 * G)] + [
                   (wq_hi[:, :, 2 * D:], wq_lo[:, :, 2 * D:], wq_raw[:, :, 2 * D:]),
                   (wp_hi[:, :, :], wp_lo[:, :, :], wp_raw)]

        @block.sync
        def _(sp):
            sp.dma_start(adj_raw, adj.rearrange("(t p) m -> p t m", p=P)).then_inc(adj_loaded, 16)
            sp.dma_start(wg_raw, w_gcn.rearrange("(c p) d -> p c d", p=P)).then_inc(w_loaded, 16)
            sp.dma_start(wp_raw, w_proj.rearrange("(c p) d -> p c d", p=P)).then_inc(w_loaded, 16)
            sp.dma_start(wq_raw, w_qkv.rearrange("(c p) d -> p c d", p=P)).then_inc(w_loaded, 16)
            for n, row in enumerate((b_gcn, b_proj)):
                sp.dma_start(bias_raw[:, n, :], row.partition_broadcast(KS)).then_inc(w_loaded, 16)
            for tile, row in ((gamma, ln_gamma), (beta, ln_beta)):
                sp.dma_start(tile[:, :], row.partition_broadcast(P)).then_inc(w_loaded, 16)

            def load_x(b, h):
                if live(b):
                    free = ahead(sp, upto(T, b, 2 * h))
                    sp.wait_ge(adj_loaded, 16)
                    wait(sp, x_split, free)
                    sp.dma_start(x_raw[:, :, :], x_v[index(b)][:, 2 * h:2 * h + 2, :]).then_inc(x_loaded, 16)

            def load_c(b, g):
                if live(b):
                    sp.wait_ge(c_rows_set, upto(G, b, g + 1))
                    for n in range(2):
                        row = q_stack[parity(b)][KS + n:KS + n + 1, g * J:(g + 1) * J, :]
                        sp.dma_start(row.rearrange("o j (t p) -> o (j t) p", p=P).bitcast(f32),
                                     c_rows[n * QUAD:(n + 1) * QUAD, :].bitcast(f32)).then_inc(c_loaded[g], 16)

            def load_stack(b, g, which):
                if live(b):
                    split = ahead(sp, upto(2 * G, b, 2 * g + which + 1))
                    free = ahead(sp, upto(2 * UNITS, minus(b, 2), (g + 1) * 2 * UNITS // G))
                    sp.wait_ge(qk_lo_set, split)
                    wait(sp, st_made, free)
                    stack = (q_stack, k_stack)[which][parity(b)]
                    done = (q_loaded, k_loaded)[which][parity(b)][g]
                    parts = ((stage_hi, stage_lo, stage_hi), (stage_hi, stage_hi, stage_lo))[which]
                    for n, part in enumerate(parts):
                        sp.dma_start(stack[n * HD:(n + 1) * HD, g * J:(g + 1) * J, :].bitcast(f32),
                                     part[:, which, :].bitcast(f32)).then_inc(done, 16)

            def store(b):
                if live(b):
                    given = ahead(sp, upto(T, b, T))
                    sp.wait_ge(adj_loaded, 16)
                    sp.wait_ge(res_set, given)
                    sp.dma_start(out_v[index(b)], res[:, :, :]).then_inc(stored, 16)

            def step(i):
                load_x(minus(i, -2), 0)
                load_c(minus(i, 1), 1)
                load_x(minus(i, -2), 1)
                load_stack(minus(i, -1), 0, 0)
                load_stack(minus(i, -1), 0, 1)
                load_c(i, 0)
                load_stack(minus(i, -1), 1, 0)
                load_stack(minus(i, -1), 1, 1)
                store(minus(i, 2))

            run(sp, step)
            sp.wait_ge(stored, 16 * B)

        @block.tensor
        def _(pe):
            def split_sum(dst, pairs, first=True):
                terms = [(a, b) for (ah, al), (bh, bl) in pairs for a, b in ((ah, bh), (al, bh), (ah, bl))]
                for n, (a, b) in enumerate(terms):
                    last = nc.tensor.matmul(dst, a, b, start=first and n == 0, stop=n == len(terms) - 1)
                return last

            pe.wait_ge(ident_made, 2)
            pe.wait_ge(adj_loaded, 16)
            for m in range(T):
                for t in range(T):
                    last = nc.tensor.transpose(ps[:, m, t * P:(t + 1) * P], adj_raw[:, t, m * P:(m + 1) * P], ident[:, :])
            last.then_inc(adj_t_made, 1)
            pe.wait_ge(const_step, T)
            for m in range(T):
                for t in range(T):
                    last = nc.tensor.transpose(ps[:, 4 + m, t * P:(t + 1) * P], adj_row[:, t, m * P:(m + 1) * P], ident[:, :])
            last.then_inc(row_t_made, 1)
            pe.wait_ge(consts_made, 1)
            pe.wait_ge(w_lo_set, len(weights))
            pe.wait_ge(ones_made, 5)

            def aggregate(b, c, half):
                if live(b):
                    if half == 0:
                        wait(pe, qk_lo_set, upto(2 * G, minus(b, 1), c + 3))
                    if c == 0:
                        pe.wait_ge(x_split, upto(T, b, 2 * half + 2))
                    cols = slice(c * P, (c + 1) * P)
                    terms = [(p, q) for t in (2 * half, 2 * half + 1)
                             for p, q in ((x_hi[:, t, cols], at_hi[:, t, :]), (x_lo[:, t, cols], at_hi[:, t, :]),
                                          (x_hi[:, t, cols], at_lo[:, t, :]))]
                    for n, (p, q) in enumerate(terms):
                        last = nc.tensor.matmul(ps[:, misc_bank(c), :], p, q, start=half == 0 and n == 0,
                                                stop=half == 1 and n == len(terms) - 1)
                    if half == 1:
                        last.then_inc(z_sum, 1)

            def gcn(b, t):
                if live(b):
                    h, n = t // 2, t % 2
                    if n == 0:
                        pe.wait_ge(z_lo_set, upto(C, b, C))
                    rows, dst = slice(t * P, (t + 1) * P), ps[:, misc_bank(h), n * D:(n + 1) * D]
                    nc.tensor.matmul(dst, bias_sel[:, :], bias_rows[:, 0, :], start=True, stop=False)
                    nc.tensor.matmul(dst, ident_r[:, :], x_hi[:, t, :], start=False, stop=False)
                    nc.tensor.matmul(dst, ident_r[:, :], x_lo[:, t, :], start=False, stop=False)
                    last = split_sum(dst, [((z_hi[:, c, rows], z_lo[:, c, rows]), (wg_hi[:, c, :], wg_lo[:, c, :]))
                                           for c in range(C)], first=False)
                    if n == 1:
                        last.then_inc(gcn_sum, 1)

            def transpose_y(b, c):
                if live(b):
                    if c == 1:
                        wait(pe, v_set, upto(2, minus(b, 1), 2))
                        pe.wait_ge(y_set, upto(T, b, T))
                    else:
                        wait(pe, o_set, upto(2, minus(b, 3), 1))
                    for t in range(T):
                        last = nc.tensor.transpose(ps[:, misc_bank(c), t * P:(t + 1) * P],
                                                   y[:, parity(b), t, c * P:(c + 1) * P], ident[:, :])
                    last.then_inc(yt_made, 1)

            def queries_keys(b, g, which):
                if live(b):
                    if g == 0 and which == 0:
                        pe.wait_ge(yt_lo_set, upto(C, b, C))
                    if g:
                        pe.wait_ge(qk_lo_set, upto(2 * G, b, which + 1))
                    elif which:
                        wait(pe, o_set, upto(2, minus(b, 3), 2))
                    cols = slice(which * D + g * P, which * D + (g + 1) * P)
                    split_sum(ps[:, misc_bank(2 * g + which), :],
                              [((wq_hi[:, c, cols], wq_lo[:, c, cols]), (yt_hi[:, c, :], yt_lo[:, c, :]))
                               for c in range(C)]).then_inc(qk_sum, 1)

            def values(b, h):
                if live(b):
                    pe.wait_ge(qk_lo_set, upto(2 * G, b, h + 3))
                    pe.wait_ge(r_set, clipped(2, minus(b, -1), h + 1))
                    for n in range(2):
                        rows = slice((2 * h + n) * P, (2 * h + n + 1) * P)
                        last = split_sum(ps[:, misc_bank(h), n * D:(n + 1) * D],
                                         [((yt_hi[:, c, rows], yt_lo[:, c, rows]),
                                           (wq_hi[:, c, 2 * D:3 * D], wq_lo[:, c, 2 * D:3 * D])) for c in range(C)])
                    last.then_inc(v_sum, 1)

            def project(b, h):
                if live(b):
                    if h == 0:
                        wait(pe, o_set, upto(2, minus(b, 1), 1))
                        pe.wait_ge(v_set, clipped(2, minus(b, -2), 1))
                    else:
                        wait(pe, o_set, upto(2, minus(b, 1), 2))
                        pe.wait_ge(v_set, clipped(2, minus(b, -2), 2))
                        pe.wait_ge(yt_lo_set, clipped(C, minus(b, -3), 1))
                    if h == 0:
                        pe.wait_ge(ot_lo_set, upto(G, b, G))
                    for n in range(2):
                        rows, dst = slice((2 * h + n) * P, (2 * h + n + 1) * P), ps[:, misc_bank(h), n * D:(n + 1) * D]
                        nc.tensor.matmul(dst, bias_sel[:, :], bias_rows[:, 1, :], start=True, stop=False)
                        last = split_sum(dst, [((ot_hi[:, c, rows], ot_lo[:, c, rows]), (wp_hi[:, c, :], wp_lo[:, c, :]))
                                               for c in range(C)], first=False)
                    last.then_inc(proj_sum, 1)

            def wait_turn(b, turn):
                before = turn - 2
                if before == 4:
                    wait(pe, c_rows_set, upto(G, minus(b, 1), 2))
                elif before == 21:
                    wait(pe, c_rows_set, upto(G, b, 1))
                else:
                    tile = before if before < 4 else before - 1 if before < 21 else before - 2
                    value = upto(TILES, b, tile + 1)
                    wait(pe, row_max, min(value, TILES * B) if isinstance(value, int) else value)

            def score(b, k):
                if live(b):
                    g, t, j = score_tile(k)
                    if k % QUAD == 0:
                        pe.wait_ge(q_loaded[parity(b)][g], upto_parity(LOADS, b, LOADS))
                        pe.wait_ge(k_loaded[parity(b)][g], upto_parity(LOADS, b, LOADS))
                    turn = k if k < 4 else k + 1 if k < 20 else k + 2
                    wait_turn(b, turn)
                    nc.tensor.matmul(ps[:, SA + turn % 2, :], q_stack[parity(b)][0:KS, g * J + j, t * P:(t + 1) * P],
                                     k_stack[parity(b)][0:KS, g * J + j, :], start=True, stop=True).then_inc(sa_made, 1)

            def transpose_c(b, g):
                if live(b):
                    turn = (21, 4)[g]
                    pe.wait_ge(c_step, upto(3 * G, b, 3 * g + 3))
                    wait_turn(minus(b, -g), turn)
                    nc.tensor.transpose(ps[0:2 * QUAD, SA + turn % 2, 0:P],
                                        c_parts[:, g, :, :].rearrange("p h c -> p (h c)").bitcast(f32),
                                        ident[:, :]).then_inc(ct_made, 1)

            def score_t(b, u):
                if live(b):
                    g, m, p = u // (2 * T), u // 2 % T, u % 2
                    if u % (2 * T) == 0:
                        pe.wait_ge(c_loaded[g], upto(32, b, 32))
                    for n in range(2):
                        h = g * J + 2 * p + n
                        bank, before = st_bank(u, n)
                        wait(pe, p_exp, upto(2 * UNITS, b, before + 1))
                        nc.tensor.matmul(ps[:, bank, :], k_stack[parity(b)][0:KC, h, m * P:(m + 1) * P],
                                         q_stack[parity(b)][0:KC, h, :], start=True, stop=True).then_inc(st_made, 1)

            def weigh(b, g, m):
                if live(b):
                    if m == 0:
                        wait(pe, ot_lo_set, upto(G, b, g))
                        pe.wait_ge(v_set, upto(2, b, 2))
                    unit = g * 2 * T + 2 * m + 1
                    if shared(b, unit):
                        pe.wait_ge(p_masked, upto(UNITS, b, 4 + (unit - 3) // 2))
                        pe.wait_ge(late_masked, (unit - 3) // 2)
                    else:
                        pe.wait_ge(p_masked, upto(UNITS, b, unit + 1))
                    for j in range(J):
                        u = 2 * m + j // 2
                        h = g * J + j
                        last = nc.tensor.matmul(ps[j * HD:(j + 1) * HD, AV, :], v[:, parity(b), m, h * HD:(h + 1) * HD],
                                                pt[:, u % PT_RING, j % 2, :], start=m == 0, stop=m == T - 1)
                    last.then_inc(av_made, 1)

            def step(i):
                first, front, back = minus(i, -2), minus(i, -1), minus(i, 2)
                for s in range(SLOTS):
                    score_t(*unit_of_slot(i, s))
                    score(i, 2 * s)
                    score(i, 2 * s + 1)
                    if s % 2 == 1:
                        n = (s - 15) % 16 // 2
                        weigh(i if s == 15 else minus(i, 1), n // T, n % T)
                    if s == 0:
                        values(i, 1)
                    if s in (1, 4):
                        project(back, s // 4)
                    if s == 3:
                        transpose_y(front, 1)
                        transpose_y(front, 0)
                    if 5 <= s < 9:
                        queries_keys(front, (s - 5) // 2, (s - 5) % 2)
                    if 8 <= s < 12:
                        aggregate(first, (s - 8) // 2, s % 2)
                    if s in (13, 14):
                        gcn(first, 2 * s - 26)
                        gcn(first, 2 * s - 25)
                    if s == 15:
                        values(front, 0)
                    if s == 1:
                        transpose_c(minus(i, 1), 1)
                    if s == 9:
                        transpose_c(i, 0)

            run(pe, step)

        @block.scalar
        def _(act):
            act.wait_ge(deg_step, 3)
            nc.scalar.activation(deg_root[:, :], deg[:, :], ACT.Sqrt).then_inc(root_made, 1)
            nc.scalar.preload_act_table_set("natural_log_exp_and_others")
            act.wait_ge(w_loaded, 16 * 7)
            for hi, _, raw in weights:
                nc.scalar.activation(hi, raw, ACT.Copy).then_inc(w_hi_set, 1)
            act.wait_ge(w_lo_set, len(weights))

            def z_hi_part(b, c):
                if live(b):
                    act.wait_ge(z_sum, upto(C, b, c + 1))
                    nc.scalar.activation(z_hi[:, c, :], ps[:, misc_bank(c), :], ACT.Copy).then_inc(z_hi_set, 1)

            def yt_hi_part(b, c):
                if live(b):
                    act.wait_ge(yt_made, upto(C, b, C - c))
                    nc.scalar.activation(yt_hi[:, c, :], ps[:, misc_bank(c), :], ACT.Copy).then_inc(yt_hi_set, 1)

            def qk_hi(b, g, which):
                if live(b):
                    act.wait_ge(qk_sum, upto(2 * G, b, 2 * g + which + 1))
                    loaded = (q_loaded, k_loaded)[which]
                    if g:
                        act.wait_ge(loaded[parity(b)][0], upto_parity(LOADS, b, LOADS))
                    else:
                        wait(act, loaded[1 - parity(b)][G - 1], upto_parity(LOADS, minus(b, 1), LOADS))
                    nc.scalar.activation(stage_hi[:, which, :], ps[:, misc_bank(2 * g + which), :], ACT.Copy,
                                         scale=(SCALE, 1.0)[which]).then_inc(qk_hi_set, 1)

            def v_copy(b, h):
                if live(b):
                    act.wait_ge(v_sum, upto(2, b, h + 1))
                    nc.scalar.activation(v[:, parity(b), 2 * h:2 * h + 2, :], ps[:, misc_bank(h), :], ACT.Copy).then_inc(v_set, 1)

            def o_copy(b, h):
                if live(b):
                    act.wait_ge(proj_sum, upto(2, b, h + 1))
                    wait(act, ln2_step, upto(LN2_STEPS, minus(b, 1), 21))
                    nc.scalar.activation(o[:, 2 * h:2 * h + 2, :], ps[:, misc_bank(h), :], ACT.Copy).then_inc(o_set, 1)

            def r_copy(b, h):
                if live(b):
                    act.wait_ge(gcn_sum, upto(2, b, h + 1))
                    wait(act, yb_set, upto(2, minus(b, 2), h + 1))
                    nc.scalar.activation(y[:, parity(b), 2 * h:2 * h + 2, :], ps[:, misc_bank(h), :],
                                         ACT.Copy).then_inc(r_set, 1)

            def ot_round(b, g):
                if live(b):
                    act.wait_ge(av_made, upto(G * T, b, (g + 1) * T))
                    wait(act, proj_sum, upto(2, b, 0))
                    nc.scalar.activation(ot_hi[:, g, :], ps[:, AV, :], ACT.Copy).then_inc(ot_hi_set, 1)

            def exp_t(b, u):
                if live(b):
                    for n in range(2):
                        act.wait_ge(st_made, upto(2 * UNITS, b, 2 * u + n + 1))
                        if n == 0:
                            wait(act, av_made, upto(G * T, b, (u - PT_RING) // 2 + 1))
                        nc.scalar.activation(pt[:, u % PT_RING, n, :], ps[:, st_bank(u, n)[0], :],
                                             ACT.Exp).then_inc(p_exp, 1)

            def exp_row(b, k):
                if live(b):
                    act.wait_ge(row_max, upto(TILES, b, k + 1))
                    col = slice(column(k), column(k) + 1)
                    nc.scalar.activation(neg_s[:, k % MS_RING, :], neg_s[:, k % MS_RING, :], ACT.Exp, bias=neg_max[:, parity(b), col],
                                         scale=-1.0, accum_out=sums[:, col]).then_inc(row_exp, 1)

            def ln_sum(b, g):
                if live(b):
                    act.wait_ge(row_exp, upto(TILES, b, (g + 1) * QUAD))
                    cols = slice(g * QUAD, (g + 1) * QUAD)
                    nc.scalar.activation(ln_sums[:, cols], sums[:, cols], ACT.Ln).then_inc(ln_sum_set, 1)

            def inverse_root(b, n):
                if live(b):
                    step_sem, root_sem, steps, k, per, at = (
                        (ln1_step, ln1_root, LN1_STEPS, 9, 2, 0), (ln2_step, ln2_root, LN2_STEPS, 9, 4, 0),
                        (ln2_step, ln2_root, LN2_STEPS, 31, 4, 2))[n]
                    act.wait_ge(step_sem, upto(steps, b, k))
                    nc.scalar.activation(root[n][:, :], var_eps[n][:, :], ACT.Ln).then_inc(root_sem, 1)
                    act.wait_ge(root_sem, upto(per, b, at + 1))
                    nc.scalar.activation(root[n][:, :], root[n][:, :], ACT.Exp, scale=-0.5).then_inc(root_sem, 1)

            def step(i):
                first, front, last, back = minus(i, -2), minus(i, -1), minus(i, 1), minus(i, 2)
                for s in range(SLOTS):
                    exp_row(i if s else last, (2 * s - 2) % TILES)
                    if s in (0, 1):
                        v_copy(i, s)
                    if s in (2, 5):
                        o_copy(back, s // 5)
                    if s == 4:
                        yt_hi_part(front, 1)
                        yt_hi_part(front, 0)
                    if 6 <= s < 10:
                        qk_hi(front, (s - 6) // 2, s % 2)
                    if s in (14, 15):
                        r_copy(first, s - 14)
                    if s in (6, 14):
                        ot_round(last, (s - 6) // 8)
                    exp_row(i if s else last, (2 * s - 1) % TILES)
                    if s in (10, 12):
                        z_hi_part(first, (s - 10) // 2)
                    if s == 1:
                        inverse_root(front, 0)
                    if s == 6:
                        inverse_root(back, 1)
                    if s == 14:
                        inverse_root(back, 2)
                    exp_t(*unit_of_slot(i, s))
                    if s == 0:
                        ln_sum(last, 1)
                    if s == 8:
                        ln_sum(i, 0)

            run(act, step)

        @block.vector
        def _(dve):
            deg_n, const_n = [0], [0]

            def deg_link(ins):
                deg_n[0] += 1
                ins.then_inc(deg_step, 1)
                dve.wait_ge(deg_step, deg_n[0])

            dve.wait_ge(adj_loaded, 16)
            deg_link(nc.vector.reduce_sum(d_inv[:, :], adj_raw, axis=AX.X))
            deg_link(nc.vector.tensor_scalar(deg_pos[:, :], d_inv[:, :], 0.0, None, ALU.is_gt))
            deg_link(nc.vector.tensor_scalar_max(deg[:, :], d_inv[:, :], 1e-30))
            nc.vector.tensor_scalar(negmask[:, :, :], adj_raw, 0.0, NEG, ALU.is_equal, ALU.mult)
            dve.wait_ge(root_made, 1)
            deg_link(nc.vector.reciprocal(d_inv[:, :], deg_root[:, :]))
            deg_link(nc.vector.tensor_tensor(deg_root[:, :], d_inv[:, :], d_inv[:, :], ALU.mult))
            deg_link(nc.vector.scalar_tensor_tensor(deg_root[:, :], deg_root[:, :], -0.5, deg[:, :], ALU.mult, ALU.mult))
            deg_link(nc.vector.scalar_tensor_tensor(d_inv[:, :], deg_root[:, :], 1.5, d_inv[:, :], ALU.add, ALU.mult))
            deg_link(nc.vector.tensor_tensor(d_inv[:, :], d_inv[:, :], deg_pos[:, :], ALU.mult))
            for t in range(T):
                nc.vector.tensor_scalar(adj_row[:, t, :], adj_raw[:, t, :], d_inv[:, t:t + 1], None,
                                        ALU.mult).then_inc(const_step, 1)
            const_n[0] = T

            dve.wait_ge(w_loaded, 16 * 7)
            nc.vector.tensor_copy(wg_hi[:, :, :], wg_raw).then_inc(const_step, 1)
            const_n[0] += 1
            dve.wait_ge(const_step, const_n[0])
            nc.vector.tensor_tensor(wg_lo[:, :, :], wg_raw, wg_hi[:, :, :].bitcast(f32), ALU.subtract)
            nc.vector.tensor_copy(bias_rows[:, :, :], bias_raw).then_inc(const_step, 1)
            const_n[0] += 1
            dve.wait_ge(const_step, const_n[0])
            nc.vector.tensor_tensor(bias_rows[HD:2 * HD, :, :], bias_raw[HD:2 * HD, :, :],
                                    bias_rows[HD:2 * HD, :, :].bitcast(f32), ALU.subtract)
            dve.wait_ge(ident_made, 2)
            nc.vector.tensor_copy(ident_r[:, :], ident[:, :])
            dve.wait_ge(adj_t_made, 1)
            nc.vector.tensor_scalar(keep_t[:, :, :], ps[:, 0:4, :], 0.0, None, ALU.not_equal)
            dve.wait_ge(row_t_made, 1)
            for m in range(T):
                nc.vector.tensor_scalar(at_hi[:, m, :], ps[:, 4 + m, :], d_inv[:, m:m + 1], None,
                                        ALU.mult).then_inc(const_step, 1)
                const_n[0] += 1
                dve.wait_ge(const_step, const_n[0])
                made = nc.vector.scalar_tensor_tensor(at_lo[:, m, :], ps[:, 4 + m, :], d_inv[:, m:m + 1],
                                                      at_hi[:, m, :].bitcast(f32), ALU.mult, ALU.subtract)
            made.then_inc(consts_made, 1)

            def split_x(b, t):
                if live(b):
                    if t == 0:
                        wait(dve, gcn_sum, upto(2, b, 0))
                    if t % 2 == 0:
                        dve.wait_ge(x_loaded, upto(32, b, 8 * t + 16))
                    raw = x_raw[:, t % 2, :]
                    nc.vector.tensor_copy(x_hi[:, t, :], raw).then_inc(x_hi_set, 1)
                    dve.wait_ge(x_hi_set, upto(T, b, t + 1))
                    nc.vector.tensor_tensor(x_lo[:, t, :], raw, x_hi[:, t, :].bitcast(f32),
                                            ALU.subtract).then_inc(x_split, 1)

            def remainder(lo, hi, bank):
                return nc.vector.tensor_tensor(lo, ps[:, bank, :], hi.bitcast(f32), ALU.subtract)

            def z_lo_part(b, c):
                if live(b):
                    dve.wait_ge(z_hi_set, upto(C, b, c + 1))
                    remainder(z_lo[:, c, :], z_hi[:, c, :], misc_bank(c)).then_inc(z_lo_set, 1)

            def yt_lo_part(b, c):
                if live(b):
                    dve.wait_ge(yt_hi_set, upto(C, b, C - c))
                    remainder(yt_lo[:, c, :], yt_hi[:, c, :], misc_bank(c)).then_inc(yt_lo_set, 1)

            def qk_lo(b, g, which):
                if live(b):
                    dve.wait_ge(qk_hi_set, upto(2 * G, b, 2 * g + which + 1))
                    nc.vector.scalar_tensor_tensor(stage_lo[:, which, :], ps[:, misc_bank(2 * g + which), :], (SCALE, 1.0)[which],
                                                   stage_hi[:, which, :].bitcast(f32), ALU.mult,
                                                   ALU.subtract).then_inc(qk_lo_set, 1)

            def ot_lo_part(b, g):
                if live(b):
                    dve.wait_ge(ot_hi_set, upto(G, b, g + 1))
                    remainder(ot_lo[:, g, :], ot_hi[:, g, :], AV).then_inc(ot_lo_set, 1)

            def c_column(b, g):
                if live(b):
                    dve.wait_ge(ln_sum_set, upto(G, b, g + 1))
                    cols = slice(g * QUAD, (g + 1) * QUAD)
                    nc.vector.tensor_tensor(c_col[:, :], neg_max[:, parity(b), cols], ln_sums[:, cols],
                                            ALU.subtract).then_inc(c_step, 1)
                    dve.wait_ge(c_step, upto(3 * G, b, 3 * g + 1))
                    nc.vector.tensor_copy(c_parts[:, g, 0, :], c_col[:, :]).then_inc(c_step, 1)
                    dve.wait_ge(c_step, upto(3 * G, b, 3 * g + 2))
                    nc.vector.tensor_tensor(c_parts[:, g, 1, :], c_col[:, :], c_parts[:, g, 0, :].bitcast(f32),
                                            ALU.subtract).then_inc(c_step, 1)

            def c_row_copy(b, g):
                if live(b):
                    dve.wait_ge(ct_made, upto(G, b, g + 1))
                    wait(dve, c_loaded[1 - g], upto(32, b, 32 * g))
                    turn = (21, 4)[g]
                    nc.vector.tensor_copy(c_rows[:, :], ps[0:2 * QUAD, SA + turn % 2, 0:P]).then_inc(c_rows_set, 1)

            def mask_and_max(b, k):
                if live(b):
                    g, t, j = score_tile(k)
                    made, free = ahead(dve, upto(TILES, b, k + 1)), ahead(dve, upto(TILES, b, k - MS_RING + 1))
                    dve.wait_ge(consts_made, 1)
                    dve.wait_ge(sa_made, made)
                    wait(dve, row_exp, free)
                    nc.vector.tensor_tensor_reduce(
                        out=neg_s[:, k % MS_RING, :], in0=ps[:, SA + (k if k < 4 else k + 1 if k < 20 else k + 2) % 2, :],
                        in1=negmask[:, t, :], scale=-1.0, scalar=3e38, op0=ALU.add, op1=ALU.min,
                        accum_out=neg_max[:, parity(b), column(k):column(k) + 1]).then_inc(row_max, 1)

            def tile_stats(n, chain, src, tiles):
                for t in tiles:
                    nc.vector.bn_stats(stats[n][:, t, :], src[:, t, :]).then_inc(chain, 1)

            def finish_stats(n, chain, per, b, k):
                given = ahead(dve, upto(per, b, k))
                dve.wait_ge(consts_made, 1)
                dve.wait_ge(chain, given)
                for t in range(T):
                    nc.vector.bn_aggr(mean_var[n][:, t, :], stats[n][:, t, :]).then_inc(chain, 1)
                dve.wait_ge(chain, upto(per, b, k + T))
                nc.vector.tensor_scalar_add(var_eps[n][:, :], mean_var[n][:, :, 1], EPS).then_inc(chain, 1)

            def newton(n, chain, per, b, k, root_sem, root_value):
                dve.wait_ge(root_sem, root_value)
                nc.vector.tensor_tensor(rstd[n][:, :], root[n][:, :], root[n][:, :], ALU.mult).then_inc(chain, 1)
                dve.wait_ge(chain, upto(per, b, k + 1))
                nc.vector.scalar_tensor_tensor(rstd[n][:, :], rstd[n][:, :], -0.5, var_eps[n][:, :], ALU.mult,
                                               ALU.mult).then_inc(chain, 1)
                dve.wait_ge(chain, upto(per, b, k + 2))
                nc.vector.scalar_tensor_tensor(rstd[n][:, :], rstd[n][:, :], 1.5, root[n][:, :], ALU.add,
                                               ALU.mult).then_inc(chain, 1)
                dve.wait_ge(chain, upto(per, b, k + 3))

            def late_mask(b, u):
                if shared(b, u) and u % 2:
                    m = u // 2 % T
                    dve.wait_ge(p_exp, upto(2 * UNITS, b, 2 * u + 2))
                    tile = pt[:, u % PT_RING, :, :].bitcast(i32)
                    nc.vector.tensor_tensor(tile, tile, keep_t[:, m:m + 1, :].to_broadcast([P, 2, N]),
                                            ALU.mult).then_inc(late_masked, 1)

            def ln1_stats(b, h):
                if live(b):
                    dve.wait_ge(r_set, upto(2, b, h + 1))
                    tile_stats(0, ln1_step, y[:, parity(b), :, :], (2 * h, 2 * h + 1))
                    if h == 1:
                        finish_stats(0, ln1_step, LN1_STEPS, b, T)

            def ln1_finish(b):
                if live(b):
                    newton(0, ln1_step, LN1_STEPS, b, 9, ln1_root, upto(2, b, 2))
                    for t in range(T):
                        tile = y[:, parity(b), t, :]
                        nc.vector.tensor_scalar(tile, tile, mean_var[0][:, t, 0:1], rstd[0][:, t:t + 1], ALU.subtract,
                                                ALU.mult).then_inc(y_set, 1)

            def ln2_stats(b, h):
                if live(b):
                    dve.wait_ge(o_set, upto(2, b, h + 1))
                    tile_stats(1, ln2_step, o[:, :, :], (2 * h, 2 * h + 1))
                    if h == 1:
                        finish_stats(1, ln2_step, LN2_STEPS, b, T)

            def ln2_rstd(b):
                if live(b):
                    newton(1, ln2_step, LN2_STEPS, b, 9, ln2_root, upto(4, b, 2))

            def ln2_add(b, h):
                if live(b):
                    if h == 0:
                        wait(dve, stored, upto(16, b, 0))
                    for n in range(2):
                        t = 2 * h + n
                        nc.vector.scalar_tensor_tensor(res[:, t, :], o[:, t, :], mean_var[1][:, t, 0:1], gamma[:, :],
                                                       ALU.subtract, ALU.mult).then_inc(ln2_step, 1)
                    for n in range(2):
                        t = 2 * h + n
                        dve.wait_ge(ln2_step, upto(LN2_STEPS, b, 12 + 5 * h + n + 1))
                        nc.vector.scalar_tensor_tensor(res[:, t, :], res[:, t, :], rstd[1][:, t:t + 1], o[:, t, :],
                                                       ALU.mult, ALU.add).then_inc(ln2_step, 1)

            def ln2_residual(b, h):
                if live(b):
                    dve.wait_ge(ln2_step, upto(LN2_STEPS, b, 16 + 5 * h))
                    dve.wait_ge(yb_set, upto(2, b, h + 1))
                    tiles = slice(2 * h, 2 * h + 2)
                    nc.vector.tensor_tensor(res[:, tiles, :], res[:, tiles, :], yb[:, parity(b), tiles, :],
                                            ALU.add).then_inc(ln2_step, 1)

            def ln3_stats(b):
                if live(b):
                    dve.wait_ge(ln2_step, upto(LN2_STEPS, b, 22))
                    tile_stats(2, ln2_step, res[:, :, :], range(T))
                    finish_stats(2, ln2_step, LN2_STEPS, b, 22 + T)

            def ln3_finish(b):
                if live(b):
                    newton(2, ln2_step, LN2_STEPS, b, 31, ln2_root, upto(4, b, 4))
                    for t in range(T):
                        nc.vector.tensor_scalar(res[:, t, :], res[:, t, :], mean_var[2][:, t, 0:1], rstd[2][:, t:t + 1],
                                                ALU.subtract, ALU.mult).then_inc(res_set, 1)

            def step(i):
                first, front, last, back = minus(i, -2), minus(i, -1), minus(i, 1), minus(i, 2)
                for s in range(SLOTS):
                    if s == 4:
                        yt_lo_part(front, 1)
                        yt_lo_part(front, 0)
                    if 6 <= s < 10:
                        qk_lo(front, (s - 6) // 2, s % 2)
                    if s == 1:
                        c_column(last, 1)
                    if s == 9:
                        c_column(i, 0)
                    if s == 2:
                        c_row_copy(last, 1)
                    if s == 10:
                        c_row_copy(i, 0)
                    if s in (6, 14):
                        ot_lo_part(last, (s - 6) // 8)
                    mask_and_max(i, 2 * s)
                    mask_and_max(i, 2 * s + 1)
                    late_mask(*unit_of_slot(i, s))
                    if s in (10, 12):
                        z_lo_part(first, (s - 10) // 2)
                    if s in (15, 0):
                        ln1_stats(first if s else front, s // 15 ^ 1)
                    if s == 2:
                        ln1_finish(front)
                    if s in (3, 5):
                        ln2_stats(back, s // 4)
                    if s == 7:
                        ln2_rstd(back)
                    if s in (8, 10):
                        ln2_add(back, s // 2 - 4)
                    if s in (9, 11):
                        ln2_residual(back, s // 2 - 4)
                    if s == 13:
                        ln3_stats(back)
                    if s == 15:
                        ln3_finish(back)
                    if s in (1, 3, 6, 7):
                        split_x(minus(i, -2), (1, 3, 6, 7).index(s))

            run(dve, step)

        @block.gpsimd
        def _(pool):
            nc.gpsimd.memset(ident[:, :], 0.0).then_inc(ident_made, 1)
            pool.wait_ge(ident_made, 1)
            nc.gpsimd.affine_select(out=ident[:, :], in_=ident[:, :], compare_op=ALU.not_equal, fill=1.0, base=0,
                                    pattern=[[-1, P]], channel_multiplier=1).then_inc(ident_made, 1)
            pool.wait_ge(ident_made, 2)
            nc.gpsimd.memset(bias_sel[:, :].bitcast(f32), 0.0).then_inc(ones_made, 1)
            ones = [k_stack[0][KS:KC, :, :], k_stack[1][KS:KC, :, :], bias_sel[0:1, :], bias_sel[HD:HD + 1, :]]
            for n, rows in enumerate(ones):
                pool.wait_ge(ones_made, n + 1)
                nc.gpsimd.memset(rows.bitcast(f32), 1.0).then_inc(ones_made, 1)
            pool.wait_ge(ones_made, 5)
            for n, (hi, lo, raw) in enumerate(weights):
                pool.wait_ge(w_hi_set, n + 1)
                nc.gpsimd.tensor_tensor(lo, raw, hi.bitcast(f32), ALU.subtract).then_inc(w_lo_set, 1)
            pool.wait_ge(consts_made, 1)

            def mask(b, u):
                if live(b) and not (shared(b, u) and u % 2):
                    m = u // 2 % T
                    pool.wait_ge(p_exp, upto(2 * UNITS, b, 2 * u + 2))
                    tile = pt[:, u % PT_RING, :, :].bitcast(i32)
                    nc.gpsimd.tensor_tensor(tile, tile, keep_t[:, m:m + 1, :].to_broadcast([P, 2, N]),
                                            ALU.mult).then_inc(p_masked, 1)

            def add_beta(b, h):
                if live(b):
                    if h == 0:
                        pool.wait_ge(y_set, upto(T, b, T))
                    wait(pool, ln2_step, upto(LN2_STEPS, minus(b, 2), 17 + 5 * h))
                    tiles = slice(2 * h, 2 * h + 2)
                    nc.gpsimd.tensor_tensor(yb[:, parity(b), tiles, :], y[:, parity(b), tiles, :],
                                            beta[:, :].unsqueeze(1).to_broadcast([P, 2, D]), ALU.add).then_inc(yb_set, 1)

            def step(i):
                for s in range(SLOTS):
                    mask(*unit_of_slot(i, s))
                    if s in (10, 12):
                        add_beta(i, s // 2 - 5)

            run(pool, step)


_INS = ['x', 'adj', 'L0_gnn_weight', 'L0_gnn_bias', 'L1_gnn_w_qkv', 'L1_gnn_w_proj', 'L1_gnn_b_proj',
        'L1_gnn_ln_gamma', 'L1_gnn_ln_beta']


def kernel(**inputs):
    import numpy as _np
    import concourse.bacc as _bacc
    from concourse import mybir as _mybir
    from concourse.bass_utils import run_bass_kernel_spmd as _run

    nc = _bacc.Bacc("TRN2", target_bir_lowering=False, num_devices=1, dynamic_dma_scratch_size=4096)
    arrays, args = {}, []
    for name in _INS:
        a = _np.ascontiguousarray(inputs[name])
        arrays[f"in_{name}"] = a
        args.append(nc.dram_tensor(f"in_{name}", a.shape, _mybir.dt.from_np(a.dtype), kind="ExternalInput").ap())
    shape = arrays["in_x"].shape
    args.append(nc.dram_tensor("out_0", shape, _mybir.dt.float32, kind="ExternalOutput").ap())
    gcn_attention_resnorm_kernel(nc, *args)
    r = _run(nc, [arrays], core_ids=[0])
    return r.results[0]["out_0"]
```
